# Optimizing a Trainium2 kernel written in Bass

```python
import numpy as np
import jax
import jax.numpy as jnp

def _softmax(x, axis=-1):
    return jax.nn.softmax(x, axis=axis)

def _gelu(x):
    return jax.nn.gelu(x, approximate=True)

def _silu(x):
    return jax.nn.silu(x)

def _sigmoid(x):
    return jax.nn.sigmoid(x)

def _layernorm(x, axis=-1, eps=1e-05):
    m = jnp.mean(x, axis=axis, keepdims=True)
    v = jnp.var(x, axis=axis, keepdims=True)
    return (x - m) / jnp.sqrt(v + eps)

def _scatter_add(tgt, idx, src, axis=0):
    return tgt.at[idx].add(src)

def _segment_sum(src, seg, n):
    return jax.ops.segment_sum(src, seg, n)
kernel_name = 'mk_adaln_ffn_d1_seqx_r8_70fc4b'

def setup_inputs(seed: int=0):
    np.random.seed(seed)
    _w = jnp.asarray

    def _rec_inputs():
        import jax
        import jax.numpy as jnp
        _rk = jax.random.key(seed)
        x = -0.000125 + 0.9999 * jax.random.normal(jax.random.fold_in(_rk, 1), (64, 32, 512), jnp.float32)
        _lenS = 32 - jax.random.randint(jax.random.fold_in(_rk, 7), (64,), 0, max(1, 32 // 4) + 1, jnp.int32)
        _lenS2 = 32 - jax.random.randint(jax.random.fold_in(_rk, 8), (64,), 0, max(1, 32 // 4) + 1, jnp.int32)
        cond_128 = 0.0061147 + 1.02565 * jax.random.normal(jax.random.fold_in(_rk, 11), (64, 128), jnp.float32)
        fside_S_0 = -0.022604 + 0.987366 * jax.random.normal(jax.random.fold_in(_rk, 12), (32,), jnp.float32)
        return (x, cond_128, fside_S_0)
    x, cond_128, fside_S_0 = _rec_inputs()

    def _L0_cond_setup():
        import jax, jax.numpy as jnp
        import numpy as np
        from jax import lax
        N, C_IN, L = (32, 32, 512)
        C_OUT, K, GROUPS = (32, 9, 4)
        C_DIM, PAD, STRIDE = (128, 4, 1)
        key = jax.random.key(seed)
        k1, k2, k3, k4, k5 = jax.random.split(key, 5)
        x = jax.random.normal(k1, (N, C_IN, L), dtype=jnp.float32)
        c = jax.random.normal(k2, (N, C_DIM), dtype=jnp.float32)
        weight = jax.random.normal(k3, (C_OUT, C_IN // GROUPS, K), dtype=jnp.float32)
        c_weight = jax.random.normal(k4, (C_OUT, C_DIM), dtype=jnp.float32)
        bias = jax.random.normal(k5, (C_OUT,), dtype=jnp.float32)
        return {'x': x, 'c': c, 'weight': weight, 'c_weight': c_weight, 'bias': bias}
    _L0_cond_all = _L0_cond_setup()
    _L0_cond_in = {k: v for k, v in _L0_cond_all.items() if k in ('weight', 'c_weight')}
    del _L0_cond_all

    def _L0_ffn_setup():
        import jax, jax.numpy as jnp
        import numpy as np
        BATCH, TOK, DIM, OUT = (4, 256, 512, 512)
        E, R, TOP_K = (8, 16, 2)
        SCALING = 16.0 / R
        key = jax.random.key(seed)
        ks = jax.random.split(key, 6)
        return {'x': jax.random.normal(ks[0], (BATCH, TOK, DIM), dtype=jnp.float32), 'W_base': jax.random.normal(ks[1], (OUT, DIM), dtype=jnp.float32) / np.sqrt(DIM), 'b_base': jax.random.normal(ks[2], (OUT,), dtype=jnp.float32) * 0.01, 'W_gate': jax.random.normal(ks[3], (E, DIM), dtype=jnp.float32) * 0.01, 'A': jax.random.normal(ks[4], (E, R, DIM), dtype=jnp.float32) / np.sqrt(DIM), 'B': jax.random.normal(ks[5], (OUT, OUT // OUT * R * 0 + R), dtype=jnp.float32)[None].repeat(E, 0) * 0.0 + jax.random.normal(ks[5], (E, OUT, R), dtype=jnp.float32) * 0.02}
    _L0_ffn_all = _L0_ffn_setup()
    _L0_ffn_in = {k: v for k, v in _L0_ffn_all.items() if k in ('W_base', 'b_base', 'W_gate', 'A', 'B')}
    del _L0_ffn_all
    return {'x': x, 'cond_128': cond_128, 'fside_S_0': fside_S_0, 'L0_cond_weight': _L0_cond_in['weight'], 'L0_cond_c_weight': _L0_cond_in['c_weight'], 'L0_ffn_W_base': _L0_ffn_in['W_base'], 'L0_ffn_b_base': _L0_ffn_in['b_base'], 'L0_ffn_W_gate': _L0_ffn_in['W_gate'], 'L0_ffn_A': _L0_ffn_in['A'], 'L0_ffn_B': _L0_ffn_in['B']}

def reference(x, cond_128, fside_S_0, L0_cond_weight, L0_cond_c_weight, L0_ffn_W_base, L0_ffn_b_base, L0_ffn_W_gate, L0_ffn_A, L0_ffn_B):
    import jax
    import jax.numpy as jnp

    def _L0_cond_ref(x, c, weight, c_weight, bias):
        import jax, jax.numpy as jnp
        import numpy as np
        from jax import lax
        N, C_IN, L = (32, 32, 512)
        C_OUT, K, GROUPS = (32, 9, 4)
        C_DIM, PAD, STRIDE = (128, 4, 1)
        out = lax.conv_general_dilated(x, weight, window_strides=(STRIDE,), padding=[(PAD, PAD)], dimension_numbers=('NCH', 'OIH', 'NCH'), feature_group_count=GROUPS)
        ctx = jnp.einsum('nd,od->no', c, c_weight)
        out = out + ctx[:, :, None] + bias[None, :, None]
        return out

    def _L0_ffn_ref(x, W_base, b_base, W_gate, A, B):
        import jax, jax.numpy as jnp
        import numpy as np
        BATCH, TOK, DIM, OUT = (4, 256, 512, 512)
        E, R, TOP_K = (8, 16, 2)
        SCALING = 16.0 / R
        result = jnp.einsum('bnd,od->bno', x, W_base) + b_base
        logits = jnp.einsum('bnd,ed->bne', x, W_gate)
        probs = jax.nn.softmax(logits.astype(jnp.float32), axis=-1)
        top_p, top_i = jax.lax.top_k(probs, TOP_K)
        top_p = top_p / jnp.sum(top_p, axis=-1, keepdims=True)
        top_p = top_p.astype(x.dtype)
        route_w = jnp.sum(jax.nn.one_hot(top_i, E, dtype=x.dtype) * top_p[..., None], axis=-2)
        h = jnp.einsum('bnd,erd->bner', x, A)
        hw = h * route_w[..., None]
        delta = jnp.einsum('bner,eor->bno', hw, B)
        return result + delta * SCALING
    x = x + _L0_ffn_ref(_L0_cond_ref(x, cond_128, L0_cond_weight, L0_cond_c_weight, fside_S_0), L0_ffn_W_base, L0_ffn_b_base, L0_ffn_W_gate, L0_ffn_A, L0_ffn_B)
    return x

_drawn_inputs = setup_inputs


def setup_inputs(seed=0):
    import zlib

    import numpy as np

    out = dict(_drawn_inputs(seed))
    spreads = {}
    factors = {'L0_ffn_b_base': 64.0}
    for name, (base, spread) in spreads.items():
        noise = np.random.default_rng([zlib.crc32(name.encode()), seed]).standard_normal(out[name].shape)
        drawn = base * np.exp(spread * noise) if base else spread * noise
        out[name] = jnp.asarray(drawn.astype(out[name].dtype))
    for name, factor in factors.items():
        out[name] = (out[name] * factor).astype(out[name].dtype)
    return out
```

```python
from contextlib import ExitStack

import concourse.bass as bass
from concourse import mybir

ALU = mybir.AluOpType
ACT = mybir.ActivationFunctionType
AX = mybir.AxisListType
F32 = mybir.dt.float32

P = 128


def build(nc, x, cond, bias, conv_w, ctx_w, w_base, b_base, w_gate, lora_a, lora_b, out):
    N, CH, L = x.shape
    _, CG, TAPS = conv_w.shape
    G = CH // CG
    COND = cond.shape[1]
    OUT = w_base.shape[0]
    E, R, _ = lora_a.shape
    ER = E * R
    PH = 4
    Q = L // PH
    T = P // CH
    TG = T * G
    TILES = N // T
    BLK = (PH + TAPS - 1) // PH
    ROWS = PH * CG
    QP = Q + 2
    OB = OUT // P
    PADW = PH * BLK + PH
    NOBODY = -3.0e38
    TAKEN = 3.0e38
    STORE_LAG = 5
    assert (Q, T, BLK, ROWS, E, ER, COND, OUT) == (P, 4, 3, 32, 8, P, P, 4 * P) and TILES % 2 == 0

    x_rows = x.rearrange("n c l -> (n c) l").rearrange("(k tg c) l -> k c tg l", tg=TG, c=CG)
    out_rows = out.rearrange("n c l -> (n c) l").rearrange("(k tg c) l -> k c tg l", tg=TG, c=CG)

    with ExitStack() as ctx:
        def sb(name, shape):
            return ctx.enter_context(nc.sbuf_tensor(name, shape, F32))

        def sem(name):
            return ctx.enter_context(nc.semaphore(name))

        def pair(name):
            return [sem(f"{name}_even"), sem(f"{name}_odd")]

        x_sb = sb("x_sb", [P, TILES, L])
        x_ph = [sb(f"x_ph{r}", [P, PH, Q]) for r in range(2)]
        win = [sb(f"win{r}", [P, TG * QP]) for r in range(2)]
        conv_sb = [sb(f"conv_sb{r}", [P, T, Q]) for r in range(2)]
        c_T = [sb(f"c_T{r}", [P, PH, P]) for r in range(2)]
        hw = [sb(f"hw{r}", [P, ER]) for r in range(2)]
        hw_T = [sb(f"hw_T{r}", [P, P]) for r in range(2)]
        out_sb = [sb(f"out_sb{r}", [P, OUT]) for r in range(2)]
        neg_max = sb("neg_max", [P, 1])
        expo = sb("expo", [P, E])
        total = sb("total", [P, 1])
        inv_total = sb("inv_total", [P, 1])
        logits = sb("logits", [P, 2 * E])
        ranked = sb("ranked", [P, E])
        top2 = sb("top2", [P, E])
        rest = sb("rest", [P, 2 * E])
        is_chosen = sb("is_chosen", [P, E])
        chosen = sb("chosen", [P, E])
        chosen_sum = sb("chosen_sum", [P, 1])
        inv_chosen = sb("inv_chosen", [P, 1])
        ident = sb("ident", [P, P])
        ones = sb("ones", [1, N])
        b_bc = sb("b_bc", [P, OUT])
        w_nat = sb("w_nat", [P, OB, L])
        a_nat = sb("a_nat", [P, L])
        gate_nat = sb("gate_nat", [E, L])
        b_nat = sb("b_nat", [P, OB, E, R])
        cond_nat = sb("cond_nat", [N, COND])
        ctxw_nat = sb("ctxw_nat", [CH, COND])
        bias_rep = sb("bias_rep", [1, G, PH, CG])
        taps_nat = sb("taps_nat", [CH, CG, TAPS])
        taps_pad = sb("taps_pad", [CH, CG, PADW])
        taps_win = sb("taps_win", [CH, BLK, PH, PH, CG])
        taps_T = sb("taps_T", [ROWS, BLK, PH, CH])
        conv_lhs = sb("conv_lhs", [P, G, PH, CG])
        w_T = sb("w_T", [P, PH, OUT])
        ag_T = sb("ag_T", [P, PH, ER + E])
        b_T = sb("b_T", [P, OUT])
        cond_T = sb("cond_T", [COND, N])
        ctxw_rep = sb("ctxw_rep", [COND, G, PH, CG])
        ctx_T = sb("ctx_T", [P, N])

        bank = [ctx.enter_context(nc.psum_tensor(f"bank{i}", [P, 512], F32)) for i in range(8)]
        conv_ps, trans_ps, low_ps, y_ps = bank[0:2], bank[2:4], bank[4:6], bank[6:8]
        H = slice(0, ER)
        LOGITS = slice(ER, ER + E)
        HW_T = slice(2 * P, 3 * P)

        x_loaded, shuffled, windowed, stored = pair("x_loaded"), pair("shuffled"), pair("windowed"), pair("stored")
        w_loaded, a_loaded, gate_loaded, b_loaded = sem("w_loaded"), sem("a_loaded"), sem("gate_loaded"), sem("b_loaded")
        ctx_loaded, taps_loaded, bb_loaded = sem("ctx_loaded"), sem("taps_loaded"), sem("bb_loaded")
        ident_step, pads_zero, preset = sem("ident_step"), sem("pads_zero"), sem("preset")
        taps_step, tap_order = sem("taps_step"), sem("tap_order")
        prep_done, prep_kept = sem("prep_done"), sem("prep_kept")
        by_phase, conv_done, conv_kept = sem("by_phase"), sem("conv_done"), sem("conv_kept")
        trans_done, c_T_ready = sem("trans_done"), sem("c_T_ready")
        low_done, exp_done, route_step, hw_ready = sem("low_done"), sem("exp_done"), sem("route_step"), sem("hw_ready")
        hw_trans_done, hw_T_ready = sem("hw_trans_done"), sem("hw_T_ready")
        y_done, out_ready, biased = sem("y_done"), sem("out_ready"), sem("biased")
        ROUTE_STEPS = 9

        block = ctx.enter_context(nc.Block())

        def tiles_in_pairs(eng, first, end, step):
            with eng.Fori(first // 2, end // 2) as half:
                step(2 * half, 0)
                step(2 * half + 1, 1)

        @block.sync
        def _(sp):
            def load_x(k, r):
                sp.dma_start(x_sb[:, k, :], x_rows[k]).then_inc(x_loaded[r], 16)

            def shuffle(k, r):
                for b in range(PH):
                    rows = win[r][ROWS + b * CG:ROWS + (b + 1) * CG, :].rearrange("c (tg j) -> c tg j", j=QP)
                    sp.dma_start(rows[:, :, 1:1 + Q], x_ph[r][:, b, :]).then_inc(shuffled[r], 16)

            def store(k, r):
                sp.wait_ge(out_ready, k + 1)
                sp.dma_start(out_rows[k], out_sb[r][:, :]).then_inc(stored[r], 16)

            def step(k, r, early=False, has_store=True, more=True):
                sp.wait_ge(by_phase, k + 1)
                if more:
                    load_x(k + 2, r)
                if has_store:
                    store(k - STORE_LAG, (r - STORE_LAG) % 2)
                if not early:
                    sp.wait_ge(conv_done, k - 1)
                shuffle(k, r)

            load_x(0, 0)
            load_x(1, 1)
            sp.wait_ge(pads_zero, 1)
            for k in range(STORE_LAG + 1):
                step(k, k % 2, early=k < 2, has_store=k >= STORE_LAG)
            tiles_in_pairs(sp, STORE_LAG + 1, TILES - 2, step)
            step(TILES - 2, 0, more=False)
            step(TILES - 1, 1, more=False)
            for k in range(TILES - STORE_LAG, TILES):
                store(k, k % 2)
            for r in range(2):
                sp.wait_ge(stored[r], 16 * TILES // 2)

        @block.gpsimd
        def _(pool):
            pool.memset(ident[:, :], 0.0).then_inc(ident_step, 1)
            pool.wait_ge(ident_step, 1)
            pool.affine_select(out=ident[:, :], in_=ident[:, :], compare_op=ALU.not_equal, fill=1.0, base=0,
                               pattern=[[-1, P]], channel_multiplier=1).then_inc(ident_step, 1)
            pool.wait_ge(ident_step, 2)
            pool.memset(ones[:, :], 1.0).then_inc(preset, 1)
            pool.wait_ge(preset, 1)

            pool.wait_ge(bb_loaded, 16)
            with pool.Fori(0, TILES) as k:
                pool.wait_ge(by_phase, k + 1)
                pool.tensor_tensor(x_sb[:, k, :], x_sb[:, k, :], b_bc[:, :], ALU.add).then_inc(biased, 1)

        @block.tensor
        def _(pe):
            pe.wait_ge(ident_step, 2)
            pe.wait_ge(ctx_loaded, 48)
            pe.transpose(bank[0][:, 0:N], cond_nat[:, :], ident[0:N, 0:N])
            pe.transpose(bank[0][:, N:N + CH], ctxw_nat[:, :], ident[0:CH, 0:CH]).then_inc(prep_done, 1)
            pe.wait_ge(prep_kept, 1)
            pe.wait_ge(preset, 1)
            pe.matmul(bank[0][:, 0:N], ctxw_rep[:, :, :, :], cond_T[:, :], start=True, stop=False)
            pe.matmul(bank[0][:, 0:N], bias_rep[:, :, :, :], ones[:, :], start=False, stop=True).then_inc(prep_done, 1)

            w_ph = w_nat[:, :, :].rearrange("p ob (q ph) -> p ob q ph", ph=PH)
            a_ph = a_nat[:, :].rearrange("p (q ph) -> p q ph", ph=PH)
            gate_ph = gate_nat[:, :].rearrange("p (q ph) -> p q ph", ph=PH)

            pe.wait_ge(a_loaded, 16)
            for ph in range(PH):
                last = pe.transpose(bank[1][:, ph * P:(ph + 1) * P], a_ph[:, :, ph], ident[:, :])
            last.then_inc(prep_done, 1)
            pe.wait_ge(gate_loaded, 16)
            for ph in range(PH):
                last = pe.transpose(bank[2][:, ph * E:(ph + 1) * E], gate_ph[:, :, ph], ident[0:E, 0:E])
            last.then_inc(prep_done, 1)
            pe.wait_ge(w_loaded, 16)
            for ph in range(PH):
                for ob in range(OB):
                    last = pe.transpose(bank[3 + ph][:, ob * P:(ob + 1) * P], w_ph[:, ob, :, ph], ident[:, :])
                last.then_inc(prep_done, 1)
            pe.wait_ge(b_loaded, 16 * OB)
            for ob in range(OB):
                last = pe.transpose(bank[7][:, ob * P:(ob + 1) * P],
                                    b_nat[:, ob, :, :].rearrange("p e r -> p (e r)"), ident[:, :])
            last.then_inc(prep_done, 1)

            def convolve(k, r, half, early=False):
                pe.wait_ge(windowed[r], 32 * (half + 1))
                if not early:
                    pe.wait_ge(conv_kept, k - 1)
                rows = win[r][0:BLK * ROWS, :].rearrange("p (t g j) -> p t g j", g=G, j=QP)
                for g in range(G):
                    last = pe.matmul(conv_ps[r][g * 32:(g + 1) * 32, :], conv_lhs[0:BLK * ROWS, g, :, :],
                                     rows[:, :, g, 1:1 + Q], start=True, stop=True)
                last.then_inc(conv_done, 1)

            def transpose_c(k, r, early=False):
                pe.wait_ge(conv_kept, k + 1)
                if not early:
                    pe.wait_ge(c_T_ready, k - 1)
                for t in range(T):
                    last = pe.transpose(trans_ps[r][:, t * P:(t + 1) * P], conv_sb[r][:, t, :], ident[:, :])
                last.then_inc(trans_done, 1)

            def low_rank(k, r, early=False):
                pe.wait_ge(c_T_ready, k + 1)
                if not early:
                    pe.wait_ge(hw_T_ready, k - 1)
                for ph in range(PH):
                    last = pe.matmul(low_ps[r][:, 0:ER + E], c_T[r][:, ph, :], ag_T[:, ph, :],
                                     start=(ph == 0), stop=(ph == PH - 1))
                last.then_inc(low_done, 1)

            def base(k, r, early=False):
                if not early:
                    pe.wait_ge(out_ready, k - 1)
                for ph in range(PH):
                    pe.matmul(y_ps[r][:, :], c_T[r][:, ph, :], w_T[:, ph, :], start=(ph == 0), stop=False)

            def transpose_hw(k, r):
                pe.wait_ge(hw_ready, k + 1)
                pe.transpose(low_ps[r][:, HW_T], hw[r][:, :], ident[:, :]).then_inc(hw_trans_done, 1)

            def experts(k, r):
                pe.wait_ge(hw_T_ready, k + 1)
                pe.matmul(y_ps[r][:, :], hw_T[r][:, :], b_T[:, :], start=False, stop=True).then_inc(y_done, 1)

            def step(k, r, half, early=False, prev=True, has_next=True, has_conv=True):
                low_rank(k, r, early)
                if prev:
                    experts(k - 1, 1 - r)
                if has_next:
                    transpose_c(k + 1, 1 - r, early and r == 0)
                base(k, r, early)
                if has_conv:
                    convolve(k + 2, r, half + 1)
                transpose_hw(k, r)

            pe.wait_ge(taps_step, 3)
            pe.wait_ge(prep_kept, 9)
            convolve(0, 0, 0, early=True)
            convolve(1, 1, 0, early=True)
            transpose_c(0, 0, early=True)
            step(0, 0, 0, early=True, prev=False)
            step(1, 1, 0, early=True)
            with pe.Fori(1, TILES // 2 - 1) as half:
                step(2 * half, 0, half)
                step(2 * half + 1, 1, half)
            step(TILES - 2, 0, TILES // 2 - 1, has_conv=False)
            step(TILES - 1, 1, TILES // 2 - 1, has_next=False, has_conv=False)
            experts(TILES - 1, 1)

        @block.scalar
        def _(act):
            act.dma_start(taps_nat[:, :, :], conv_w).then_inc(taps_loaded, 16)
            act.dma_start(cond_nat[:, :], cond).then_inc(ctx_loaded, 16)
            act.dma_start(ctxw_nat[:, :], ctx_w).then_inc(ctx_loaded, 16)
            bias_src = bias.rearrange("(a g s o) -> a g s o", a=1, g=G, s=1).to_broadcast([1, G, PH, CG])
            act.dma_start(bias_rep[:, :, :, :], bias_src).then_inc(ctx_loaded, 16)
            act.dma_start(a_nat[:, :], lora_a.rearrange("e r l -> (e r) l")).then_inc(a_loaded, 16)
            act.dma_start(gate_nat[:, :], w_gate).then_inc(gate_loaded, 16)
            act.dma_start(w_nat[:, :, :], w_base.rearrange("(ob p) l -> p ob l", p=P)).then_inc(w_loaded, 16)
            act.dma_start(b_bc[:, :], b_base.rearrange("(a o) -> a o", a=1).to_broadcast([P, OUT])).then_inc(bb_loaded, 16)
            for ob in range(OB):
                act.dma_start(b_nat[:, ob, :, :],
                              lora_b[:, ob * P:(ob + 1) * P, :].rearrange("e p r -> p e r")).then_inc(b_loaded, 16)

            def shift_window(k, r, half):
                act.wait_ge(shuffled[r], 16 * PH * (half + 1))
                act.dma_start(win[r][0:ROWS, 1:], win[r][ROWS:2 * ROWS, :-1]).then_inc(windowed[r], 16)
                act.dma_start(win[r][2 * ROWS:3 * ROWS, :-1], win[r][ROWS:2 * ROWS, 1:]).then_inc(windowed[r], 16)

            shift_window(0, 0, 0)
            shift_window(1, 1, 0)

            act.wait_ge(prep_done, 1)
            act.copy(cond_T[:, :], bank[0][:, 0:N])
            cw = bank[0][:, N:N + CH].rearrange("d (g s o) -> d g s o", g=G, s=1).to_broadcast([COND, G, PH, CG])
            act.copy(ctxw_rep[:, :, :, :], cw).then_inc(prep_kept, 1)
            act.wait_ge(prep_done, 2)
            act.copy(ctx_T[:, :], bank[0][:, 0:N]).then_inc(prep_kept, 1)
            act.wait_ge(prep_done, 3)
            act.copy(ag_T[:, :, 0:ER], bank[1][:, :].rearrange("q (ph e) -> q ph e", ph=PH)).then_inc(prep_kept, 1)
            act.wait_ge(prep_done, 4)
            act.copy(ag_T[:, :, ER:ER + E], bank[2][:, 0:PH * E].rearrange("q (ph e) -> q ph e", ph=PH)).then_inc(prep_kept, 1)
            for ph in range(PH):
                act.wait_ge(prep_done, 5 + ph)
                act.copy(w_T[:, ph, :], bank[3 + ph][:, :]).then_inc(prep_kept, 1)
            act.wait_ge(prep_done, 5 + PH)
            act.copy(b_T[:, :], bank[7][:, :]).then_inc(prep_kept, 1)

            def exponentials(k, r):
                act.wait_ge(route_step, ROUTE_STEPS * k + 2)
                act.activation(expo[:, :], low_ps[r][:, LOGITS], ACT.Exp, bias=neg_max[:, :],
                               accum_out=total[:, :]).then_inc(exp_done, 1)

            def keep_c_T(k, r):
                act.wait_ge(trans_done, k + 1)
                src = trans_ps[r][:, :].rearrange("q (tg ph o) -> q ph o tg", ph=PH, o=CG)
                act.copy(c_T[r][:, :, :].rearrange("q ph (o tg) -> q ph o tg", o=CG), src).then_inc(c_T_ready, 1)

            def keep_hw_T(k, r, early=False):
                act.wait_ge(hw_trans_done, k + 1)
                if not early:
                    act.wait_ge(y_done, k - 1)
                act.copy(hw_T[r][:, :], low_ps[r][:, HW_T]).then_inc(hw_T_ready, 1)

            def step(k, r, half, early=False, has_next=True, has_conv=True):
                exponentials(k, r)
                if has_conv:
                    shift_window(k + 2, r, half + 1)
                if has_next:
                    keep_c_T(k + 1, 1 - r)
                keep_hw_T(k, r, early)

            keep_c_T(0, 0)
            step(0, 0, 0, early=True)
            step(1, 1, 0, early=True)
            with act.Fori(1, TILES // 2 - 1) as half:
                step(2 * half, 0, half)
                step(2 * half + 1, 1, half)
            step(TILES - 2, 0, TILES // 2 - 1, has_conv=False)
            step(TILES - 1, 1, TILES // 2 - 1, has_next=False, has_conv=False)

        @block.vector
        def _(dve):
            def split_phases(k, r, half, early=False):
                dve.wait_ge(x_loaded[r], 16 * (half + 1))
                if not early:
                    dve.wait_ge(shuffled[r], 16 * PH * half)
                dve.tensor_copy(x_ph[r][:, :, :], x_sb[:, k, :].rearrange("p (q ph) -> p ph q", ph=PH)).then_inc(by_phase, 1)

            def keep_conv(k, r, early=False):
                dve.wait_ge(conv_done, k + 1)
                if not early:
                    dve.wait_ge(trans_done, k - 1)
                add = ctx_T[:, bass.ds(T * k, T)].unsqueeze(2).to_broadcast([P, T, Q])
                dve.tensor_tensor(conv_sb[r][:, :, :], conv_ps[r][:, :].rearrange("p (t q) -> p t q", t=T), add,
                                  ALU.add).then_inc(conv_kept, 1)

            def route(k, r, early=False):
                def step_done(n):
                    dve.wait_ge(route_step, ROUTE_STEPS * k + n)

                def did(ins):
                    ins.then_inc(route_step, 1)

                dve.wait_ge(low_done, k + 1)
                did(dve.tensor_copy(logits[:, 0:E], low_ps[r][:, LOGITS]))
                step_done(1)
                did(dve.tensor_reduce(neg_max[:, :], logits[:, 0:E], AX.X, ALU.max, negate=True))
                did(dve.max(ranked[:, :], logits[:, 0:E]))
                step_done(3)
                did(dve.tensor_copy(top2[:, 0:2], ranked[:, 0:2]))
                dve.wait_ge(exp_done, k + 1)
                step_done(4)
                did(dve.reciprocal(inv_total[:, :], total[:, :]))
                did(dve.match_replace(rest[:, :], top2[:, :], logits[:, :], TAKEN))
                step_done(6)
                did(dve.tensor_tensor(is_chosen[:, :], logits[:, 0:E], rest[:, 0:E], ALU.not_equal))
                step_done(7)
                did(dve.scalar_tensor_tensor(out=chosen[:, :], in0=expo[:, :], scalar=inv_total[:, :],
                                             in1=is_chosen[:, :], op0=ALU.mult, op1=ALU.mult,
                                             accum_out=chosen_sum[:, :]))
                step_done(8)
                did(dve.reciprocal(inv_chosen[:, :], chosen_sum[:, :]))
                step_done(9)
                if not early:
                    dve.wait_ge(hw_trans_done, k - 1)
                dve.scalar_tensor_tensor(
                    out=hw[r][:, :].rearrange("p (e r) -> p e r", e=E),
                    in0=low_ps[r][:, H].rearrange("p (e r) -> p e r", e=E), scalar=inv_chosen[:, :],
                    in1=chosen[:, :].unsqueeze(2).to_broadcast([P, E, R]), op0=ALU.mult, op1=ALU.mult).then_inc(hw_ready, 1)

            def finish(k, r, half, early=False):
                dve.wait_ge(y_done, k + 1)
                dve.wait_ge(biased, k + 1)
                if not early:
                    dve.wait_ge(stored[r], 16 * half)
                dve.tensor_tensor(out_sb[r][:, :], y_ps[r][:, :], x_sb[:, k, :], ALU.add).then_inc(out_ready, 1)

            def step(k, r, half, early=False, early_finish=False, prev=True, has_next=True, has_x=True):
                if has_next:
                    keep_conv(k + 1, 1 - r, early and r == 0)
                route(k, r, early)
                if prev:
                    finish(k - 1, 1 - r, half - 1 + r, early or early_finish)
                if has_x:
                    split_phases(k + 4, r, half + 2)

            for r in range(2):
                edges = win[r][ROWS:2 * ROWS, :].rearrange("p (tg j) -> p tg j", j=QP)
                dve.memset(edges[:, :, 0:1], 0.0)
                last = dve.memset(edges[:, :, QP - 1:QP], 0.0)
            last.then_inc(pads_zero, 1)
            dve.memset(taps_pad[:, :, :], 0.0).then_inc(taps_step, 1)
            dve.memset(logits[:, :], NOBODY).then_inc(taps_step, 1)
            dve.memset(top2[:, :], NOBODY)
            split_phases(0, 0, 0, early=True)
            split_phases(1, 1, 0, early=True)

            dve.wait_ge(taps_loaded, 16)
            dve.wait_ge(taps_step, 2)
            dve.tensor_copy(taps_pad[:, :, PH - 1:PH - 1 + TAPS], taps_nat[:, :, :]).then_inc(tap_order, 1)
            dve.wait_ge(tap_order, 1)
            for ph in range(PH):
                src = taps_pad[:, :, PH - 1 - ph:PH - 1 - ph + BLK * PH].rearrange("o c (a b) -> o a b c", a=BLK)
                last = dve.tensor_copy(taps_win[:, :, ph, :, :], src)
            last.then_inc(tap_order, 1)
            dve.wait_ge(tap_order, 2)
            dve.transpose(taps_T[:, :, :, :].rearrange("p a h o -> p (a h o)"),
                          taps_win[:, :, :, :, :].rearrange("o a h b c -> o (a h b c)")).then_inc(tap_order, 1)
            dve.wait_ge(tap_order, 3)
            for a in range(BLK):
                src = taps_T[:, a, :, :].rearrange("p h (g o) -> p g h o", g=G)
                last = dve.tensor_copy(conv_lhs[a * ROWS:(a + 1) * ROWS, :, :, :], src)
            last.then_inc(taps_step, 1)

            split_phases(2, 0, 1)
            split_phases(3, 1, 1)
            dve.wait_ge(prep_kept, 2)
            keep_conv(0, 0, early=True)
            step(0, 0, 0, early=True, prev=False)
            step(1, 1, 0, early=True)
            step(2, 0, 1, early_finish=True)
            step(3, 1, 1)
            with dve.Fori(2, TILES // 2 - 2) as half:
                step(2 * half, 0, half)
                step(2 * half + 1, 1, half)
            step(TILES - 4, 0, TILES // 2 - 2, has_x=False)
            step(TILES - 3, 1, TILES // 2 - 2, has_x=False)
            step(TILES - 2, 0, TILES // 2 - 1, has_x=False)
            step(TILES - 1, 1, TILES // 2 - 1, has_next=False, has_x=False)
            finish(TILES - 1, 1, TILES // 2 - 1)


_INS = ["x", "cond_128", "fside_S_0", "L0_cond_weight", "L0_cond_c_weight", "L0_ffn_W_base", "L0_ffn_b_base",
        "L0_ffn_W_gate", "L0_ffn_A", "L0_ffn_B"]


def kernel(**inputs):
    import numpy as _np
    import concourse.bacc as _bacc
    from concourse.bass_utils import run_bass_kernel_spmd as _run

    nc = _bacc.Bacc("TRN2", target_bir_lowering=False, num_devices=1)
    arrays, args = {}, []
    for name in _INS:
        a = _np.ascontiguousarray(inputs[name])
        arrays[f"in_{name}_dram"] = a
        args.append(nc.dram_tensor(f"in_{name}_dram", a.shape, mybir.dt.from_np(a.dtype), kind="ExternalInput").ap())
    shape = inputs["x"].shape
    args.append(nc.dram_tensor("out_0_dram", shape, F32, kind="ExternalOutput").ap())
    build(nc, *args)
    r = _run(nc, [arrays], core_ids=[0])
    return r.results[0]["out_0_dram"]
```

```python
from contextlib import ExitStack

import concourse.bass as bass
from concourse import mybir

ALU = mybir.AluOpType
ACT = mybir.ActivationFunctionType
AX = mybir.AxisListType
F32 = mybir.dt.float32
F32R = mybir.dt.float32r

P = 128


class Tile:

    def __init__(self, j, round=0, unroll=4):
        self.j, self.round, self.unroll = j, round, unroll
        self.k = unroll * round + j
        self.parity, self.slot = j % 2, j % 4
        self.before = unroll // 2 * round + j // 2
        self.laps = unroll // 4 * round + j // 4

    def after(self, n):
        return Tile(self.j + n, self.round, self.unroll)

    def exists(self, tiles):
        return not isinstance(self.k, int) or 0 <= self.k < tiles


def for_tiles(eng, step, tiles, loop_first, rounds, unroll):
    for k in range(loop_first):
        step(Tile(k))
    with eng.Fori(0, rounds) as round:
        for j in range(unroll):
            step(Tile(loop_first + j, round, unroll))
    for k in range(loop_first + rounds * unroll, tiles):
        step(Tile(k))


def wait(eng, semaphore, value):
    if not isinstance(value, int) or value > 0:
        eng.wait_ge(semaphore, value)


def build(nc, x, cond, bias, conv_w, ctx_w, w_base, b_base, w_gate, lora_a, lora_b, out):
    N, CH, L = x.shape
    _, CG, TAPS = conv_w.shape
    G = CH // CG
    COND = cond.shape[1]
    OUT = w_base.shape[0]
    E, R, _ = lora_a.shape
    ER = E * R
    PH = 4
    Q = L // PH
    T = P // CH
    TG = T * G
    TILES = N // T
    BLK = (PH + TAPS - 1) // PH
    ROWS = PH * CG
    QP = Q + 2
    OB = OUT // P
    PADW = PH * BLK + PH
    NOBODY = -3.0e38
    TAKEN = 3.0e38
    EARLY = 2
    STORE_LAG = 5
    assert (Q, T, BLK, ROWS, E, ER, COND, OUT) == (P, 4, 3, 32, 8, P, P, 4 * P) and TILES % 2 == 0

    x_rows = x.rearrange("n c l -> (n c) l").rearrange("(k tg c) l -> k c tg l", tg=TG, c=CG)
    out_rows = out.rearrange("n c l -> (n c) l").rearrange("(k tg c) l -> k c tg l", tg=TG, c=CG)

    with ExitStack() as ctx:
        def sb(name, shape, dtype=F32):
            return ctx.enter_context(nc.sbuf_tensor(name, shape, dtype))

        def sem(name):
            return ctx.enter_context(nc.semaphore(name))

        def pair(name):
            return [sem(f"{name}_even"), sem(f"{name}_odd")]

        x_sb = sb("x_sb", [P, TILES, L])
        x_ph = [sb(f"x_ph{r}", [P, PH, Q]) for r in range(2)]
        win = [sb(f"win{r}", [P, TG * QP]) for r in range(4)]
        conv_sb = [sb(f"conv_sb{r}", [P, T, Q]) for r in range(2)]
        c_T = [sb(f"c_T{r}", [P, PH, P]) for r in range(2)]
        c_hi = [sb(f"c_hi{r}", [P, PH, P], F32R) for r in range(2)]
        c_lo = [sb(f"c_lo{r}", [P, PH, P], F32R) for r in range(2)]
        hw = [sb(f"hw{r}", [P, ER]) for r in range(2)]
        hw_hi = [sb(f"hw_hi{r}", [P, P], F32R) for r in range(2)]
        hw_lo = [sb(f"hw_lo{r}", [P, P], F32R) for r in range(2)]
        out_sb = [sb(f"out_sb{r}", [P, OUT]) for r in range(2)]
        neg_max = sb("neg_max", [P, 1])
        expo = sb("expo", [P, E])
        total = sb("total", [P, 1])
        inv_total = sb("inv_total", [P, 1])
        logits = sb("logits", [P, 2 * E])
        ranked = sb("ranked", [P, E])
        top2 = sb("top2", [P, E])
        rest = sb("rest", [P, 2 * E])
        is_chosen = sb("is_chosen", [P, E])
        chosen = sb("chosen", [P, E])
        chosen_sum = sb("chosen_sum", [P, 1])
        inv_chosen = sb("inv_chosen", [P, 1])
        ident = sb("ident", [P, P])
        ones = sb("ones", [1, N])
        b_bc = sb("b_bc", [P, OUT])
        w_nat = sb("w_nat", [P, OB, L])
        a_nat = sb("a_nat", [P, L])
        gate_nat = sb("gate_nat", [E, L])
        b_nat = sb("b_nat", [P, E, OB, R])
        b_ob = sb("b_ob", [P, OB, E, R])
        cond_nat = sb("cond_nat", [N, COND])
        ctxw_nat = sb("ctxw_nat", [CH, COND])
        bias_rep = sb("bias_rep", [1, G, PH, CG])
        taps_nat = sb("taps_nat", [CH, CG, TAPS])
        taps_pad = sb("taps_pad", [CH, CG, PADW])
        taps_win = sb("taps_win", [CH, BLK, PH, PH, CG])
        taps_T = sb("taps_T", [ROWS, BLK, PH, CH])
        conv_lhs = sb("conv_lhs", [P, G, PH, CG])
        w_hi = sb("w_hi", [P, PH, OUT], F32R)
        w_lo = sb("w_lo", [P, PH, OUT], F32R)
        ag_T = sb("ag_T", [P, PH, ER + E])
        b_hi = sb("b_hi", [P, OUT], F32R)
        b_lo = sb("b_lo", [P, OUT], F32R)
        cond_T = sb("cond_T", [COND, N])
        ctxw_rep = sb("ctxw_rep", [COND, G, PH, CG])
        ctx_T = sb("ctx_T", [P, N])

        bank = [ctx.enter_context(nc.psum_tensor(f"bank{i}", [P, 512], F32)) for i in range(8)]
        conv_ps, trans_ps, low_ps, y_ps = bank[0:2], bank[2:4], bank[4:6], bank[6:8]
        W_BANKS, B_BANK = (5, 6, 7, 5), 6
        H = slice(0, ER)
        LOGITS = slice(ER, ER + E)
        HW_T = slice(2 * P, 3 * P)

        x_loaded, shuffled, stored = pair("x_loaded"), pair("shuffled"), pair("stored")
        windowed = [sem(f"windowed{r}") for r in range(4)]
        windowed_early = [sem(f"windowed_early{r}") for r in range(EARLY)]
        w_loaded, a_loaded, gate_loaded, b_loaded = sem("w_loaded"), sem("a_loaded"), sem("gate_loaded"), sem("b_loaded")
        b_ordered = sem("b_ordered")
        ctx_loaded, taps_loaded, bb_loaded = sem("ctx_loaded"), sem("taps_loaded"), sem("bb_loaded")
        ident_step, pads_zero, preset = sem("ident_step"), sem("pads_zero"), sem("preset")
        taps_step, tap_order = sem("taps_step"), sem("tap_order")
        prep_done, prep_kept = sem("prep_done"), sem("prep_kept")
        prep_lo = sem("prep_lo")
        by_phase, conv_done, conv_kept = sem("by_phase"), sem("conv_done"), sem("conv_kept")
        trans_done, c_T_ready = sem("trans_done"), sem("c_T_ready")
        c_hi_ready, c_lo_ready = sem("c_hi_ready"), sem("c_lo_ready")
        low_done, exp_done, route_step, hw_ready = sem("low_done"), sem("exp_done"), sem("route_step"), sem("hw_ready")
        hw_trans_done, hw_hi_ready, hw_lo_ready = sem("hw_trans_done"), sem("hw_hi_ready"), sem("hw_lo_ready")
        y_done, out_ready, biased = sem("y_done"), sem("out_ready"), sem("biased")
        ROUTE_STEPS = 9

        block = ctx.enter_context(nc.Block())

        def is_early(t):
            return isinstance(t.k, int) and t.k < EARLY

        def shift_window(eng, t):
            w, done = win[t.slot], windowed_early[t.slot] if is_early(t) else windowed[t.slot]
            eng.dma_start(w[0:ROWS, 1:], w[ROWS:2 * ROWS, :-1]).then_inc(done, 16)
            eng.dma_start(w[2 * ROWS:3 * ROWS, :-1], w[ROWS:2 * ROWS, 1:]).then_inc(done, 16)

        @block.sync
        def _(sp):
            def load_x(t):
                sp.dma_start(x_sb[:, t.k, :], x_rows[t.k]).then_inc(x_loaded[t.parity], 16)

            def shuffle(t):
                wait(sp, conv_done, t.k - 3)
                for b in range(PH):
                    rows = win[t.slot][ROWS + b * CG:ROWS + (b + 1) * CG, :].rearrange("c (tg j) -> c tg j", j=QP)
                    sp.dma_start(rows[:, :, 1:1 + Q], x_ph[t.parity][:, b, :]).then_inc(shuffled[t.parity], 16)

            def store(t):
                sp.wait_ge(out_ready, t.k + 1)
                sp.dma_start(out_rows[t.k], out_sb[t.parity][:, :]).then_inc(stored[t.parity], 16)

            def step(t):
                sp.wait_ge(by_phase, t.k + 1)
                if t.after(2).exists(TILES):
                    load_x(t.after(2))
                if t.after(-STORE_LAG).exists(TILES):
                    store(t.after(-STORE_LAG))
                shuffle(t)
                if is_early(t) and not is_early(t.after(1)):
                    for k in range(EARLY):
                        sp.wait_ge(shuffled[Tile(k).parity], 16 * PH)
                        shift_window(sp, Tile(k))

            load_x(Tile(0))
            load_x(Tile(1))
            sp.wait_ge(pads_zero, 1)
            for_tiles(sp, step, TILES, loop_first=STORE_LAG + 1, rounds=2, unroll=4)
            for k in range(TILES - STORE_LAG, TILES):
                store(Tile(k))
            for r in range(2):
                sp.wait_ge(stored[r], 16 * TILES // 2)

        @block.gpsimd
        def _(pool):
            pool.memset(ident[:, :], 0.0).then_inc(ident_step, 1)
            pool.wait_ge(ident_step, 1)
            pool.affine_select(out=ident[:, :], in_=ident[:, :], compare_op=ALU.not_equal, fill=1.0, base=0,
                               pattern=[[-1, P]], channel_multiplier=1).then_inc(ident_step, 1)
            pool.wait_ge(ident_step, 2)
            pool.memset(ones[:, :], 1.0).then_inc(preset, 1)
            pool.wait_ge(preset, 1)
            pool.dma_start(cond_nat[:, :], cond).then_inc(ctx_loaded, 16)
            pool.dma_start(ctxw_nat[:, :], ctx_w).then_inc(ctx_loaded, 16)
            bias_src = bias.rearrange("(a g s o) -> a g s o", a=1, g=G, s=1).to_broadcast([1, G, PH, CG])
            pool.dma_start(bias_rep[:, :, :, :], bias_src).then_inc(ctx_loaded, 16)
            pool.dma_start(gate_nat[:, :], w_gate).then_inc(gate_loaded, 16)
            pool.dma_start(b_nat[:, :, :, :], lora_b.rearrange("e (p ob) r -> p e (ob r)", ob=OB)).then_inc(b_loaded, 16)
            pool.dma_start(b_bc[:, :], b_base.rearrange("(a o) -> a o", a=1).to_broadcast([P, OUT])).then_inc(bb_loaded, 16)
            pool.wait_ge(bb_loaded, 16)

            def step(t):
                pool.wait_ge(by_phase, t.k + 1)
                pool.wait_ge(shuffled[t.parity], 16 * PH * (t.before + 1))
                pool.tensor_tensor(x_sb[:, t.k, :], x_sb[:, t.k, :], b_bc[:, :], ALU.add).then_inc(biased, 1)
                if not is_early(t):
                    shift_window(pool, t)

            for_tiles(pool, step, TILES, loop_first=4, rounds=3, unroll=4)

        @block.tensor
        def _(pe):
            pe.wait_ge(ident_step, 2)
            w_ph = w_nat[:, :, :].rearrange("p ob (q ph) -> p ob q ph", ph=PH)
            a_ph = a_nat[:, :].rearrange("p (q ph) -> p q ph", ph=PH)
            gate_ph = gate_nat[:, :].rearrange("p (q ph) -> p q ph", ph=PH)

            pe.wait_ge(a_loaded, 16)
            for ph in range(PH):
                last = pe.transpose(bank[3][:, ph * P:(ph + 1) * P], a_ph[:, :, ph], ident[:, :])
            last.then_inc(prep_done, 1)
            pe.wait_ge(gate_loaded, 16)
            for ph in range(PH):
                last = pe.transpose(bank[4][:, ph * E:(ph + 1) * E], gate_ph[:, :, ph], ident[0:E, 0:E])
            last.then_inc(prep_done, 1)
            pe.wait_ge(w_loaded, 16)
            for ph in range(PH):
                if ph == 3:
                    pe.wait_ge(prep_lo, 1)
                for ob in range(OB):
                    last = pe.transpose(bank[W_BANKS[ph]][:, ob * P:(ob + 1) * P], w_ph[:, ob, :, ph], ident[:, :])
                last.then_inc(prep_done, 1)

            pe.wait_ge(ctx_loaded, 48)
            pe.transpose(bank[2][:, 0:N], cond_nat[:, :], ident[0:N, 0:N])
            pe.transpose(bank[2][:, N:N + CH], ctxw_nat[:, :], ident[0:CH, 0:CH]).then_inc(prep_done, 1)
            pe.wait_ge(prep_kept, 7)
            pe.wait_ge(preset, 1)
            pe.matmul(bank[2][:, 0:N], ctxw_rep[:, :, :, :], cond_T[:, :], start=True, stop=False)
            pe.matmul(bank[2][:, 0:N], bias_rep[:, :, :, :], ones[:, :], start=False, stop=True).then_inc(prep_done, 1)

            def transpose_b():
                pe.wait_ge(b_ordered, 1)
                pe.wait_ge(prep_lo, 2)
                for ob in range(OB):
                    last = pe.transpose(bank[B_BANK][:, ob * P:(ob + 1) * P], b_ob[:, ob, :, :], ident[:, :])
                last.then_inc(prep_done, 1)

            def convolve(t):
                if is_early(t):
                    pe.wait_ge(windowed_early[t.slot], 32)
                else:
                    pe.wait_ge(windowed[t.slot], 32 * (t.laps + 1 - (t.slot < EARLY)))
                wait(pe, conv_kept, t.k - 1)
                rows = win[t.slot][0:BLK * ROWS, :].rearrange("p (t g j) -> p t g j", g=G, j=QP)
                for g in range(G):
                    last = pe.matmul(conv_ps[t.parity][g * 32:(g + 1) * 32, :], conv_lhs[0:BLK * ROWS, g, :, :],
                                     rows[:, :, g, 1:1 + Q], start=True, stop=True)
                last.then_inc(conv_done, 1)

            def transpose_c(t):
                pe.wait_ge(conv_kept, t.k + 1)
                wait(pe, c_hi_ready, t.k - 1)
                wait(pe, c_lo_ready, t.k - 1)
                for s in range(T):
                    last = pe.transpose(trans_ps[t.parity][:, s * P:(s + 1) * P], conv_sb[t.parity][:, s, :], ident[:, :])
                last.then_inc(trans_done, 1)

            def low_rank(t):
                pe.wait_ge(c_T_ready, t.k + 1)
                wait(pe, hw_lo_ready, t.k - 1)
                for ph in range(PH):
                    last = pe.matmul(low_ps[t.parity][:, 0:ER + E], c_T[t.parity][:, ph, :], ag_T[:, ph, :],
                                     start=(ph == 0), stop=(ph == PH - 1))
                last.then_inc(low_done, 1)

            def base(t):
                y, hi, lo = y_ps[t.parity], c_hi[t.parity], c_lo[t.parity]
                wait(pe, out_ready, t.k - 1)
                pe.wait_ge(c_hi_ready, t.k + 1)
                for ph in range(PH):
                    pe.matmul(y[:, :], hi[:, ph, :], w_hi[:, ph, :], start=(ph == 0), stop=False)
                    pe.matmul(y[:, :], hi[:, ph, :], w_lo[:, ph, :], start=False, stop=False)
                pe.wait_ge(c_lo_ready, t.k + 1)
                for ph in range(PH):
                    pe.matmul(y[:, :], lo[:, ph, :], w_hi[:, ph, :], start=False, stop=False)

            def transpose_hw(t):
                pe.wait_ge(hw_ready, t.k + 1)
                pe.transpose(low_ps[t.parity][:, HW_T], hw[t.parity][:, :], ident[:, :]).then_inc(hw_trans_done, 1)

            def experts(t):
                y, hi, lo = y_ps[t.parity], hw_hi[t.parity], hw_lo[t.parity]
                pe.wait_ge(hw_hi_ready, t.k + 1)
                pe.matmul(y[:, :], hi[:, :], b_hi[:, :], start=False, stop=False)
                pe.matmul(y[:, :], hi[:, :], b_lo[:, :], start=False, stop=False)
                pe.wait_ge(hw_lo_ready, t.k + 1)
                pe.matmul(y[:, :], lo[:, :], b_hi[:, :], start=False, stop=True).then_inc(y_done, 1)

            def step(t):
                low_rank(t)
                if t.after(-1).exists(TILES):
                    experts(t.after(-1))
                if t.after(1).exists(TILES):
                    transpose_c(t.after(1))
                base(t)
                if t.after(2).exists(TILES):
                    convolve(t.after(2))
                transpose_hw(t)

            pe.wait_ge(taps_step, 3)
            convolve(Tile(0))
            transpose_b()
            transpose_c(Tile(0))
            convolve(Tile(1))
            pe.wait_ge(prep_kept, 9)
            pe.wait_ge(prep_lo, 5)
            for_tiles(pe, step, TILES, loop_first=2, rounds=3, unroll=4)
            experts(Tile(TILES - 1))

        @block.scalar
        def _(act):
            act.dma_start(taps_nat[:, :, :], conv_w).then_inc(taps_loaded, 16)
            act.dma_start(a_nat[:, :], lora_a.rearrange("e r l -> (e r) l")).then_inc(a_loaded, 16)
            act.dma_start(w_nat[:, :, :], w_base.rearrange("(ob p) l -> p ob l", p=P)).then_inc(w_loaded, 16)

            act.wait_ge(prep_done, 1)
            act.copy(ag_T[:, :, 0:ER], bank[3][:, :].rearrange("q (ph e) -> q ph e", ph=PH)).then_inc(prep_kept, 1)
            act.wait_ge(prep_done, 2)
            act.copy(ag_T[:, :, ER:ER + E], bank[4][:, 0:PH * E].rearrange("q (ph e) -> q ph e", ph=PH)).then_inc(prep_kept, 1)
            for ph in range(PH):
                act.wait_ge(prep_done, 3 + ph)
                act.copy(w_hi[:, ph, :], bank[W_BANKS[ph]][:, :]).then_inc(prep_kept, 1)
            act.wait_ge(prep_done, 7)
            act.copy(cond_T[:, :], bank[2][:, 0:N])
            cw = bank[2][:, N:N + CH].rearrange("d (g s o) -> d g s o", g=G, s=1).to_broadcast([COND, G, PH, CG])
            act.copy(ctxw_rep[:, :, :, :], cw).then_inc(prep_kept, 1)
            act.wait_ge(prep_done, 8)
            act.copy(ctx_T[:, :], bank[2][:, 0:N]).then_inc(prep_kept, 1)
            act.wait_ge(b_loaded, 16)
            act.copy(b_ob[:, :, :, :], b_nat[:, :, :, :].rearrange("p e ob r -> p ob e r")).then_inc(b_ordered, 1)
            act.wait_ge(prep_done, 9)
            act.copy(b_hi[:, :].rearrange("k (p ob) -> k ob p", ob=OB),
                     bank[B_BANK][:, :].rearrange("k (ob p) -> k ob p", ob=OB)).then_inc(prep_kept, 1)

            def exponentials(t):
                act.wait_ge(route_step, ROUTE_STEPS * t.k + 2)
                act.activation(expo[:, :], low_ps[t.parity][:, LOGITS], ACT.Exp, bias=neg_max[:, :],
                               accum_out=total[:, :]).then_inc(exp_done, 1)

            def keep_c(t):
                act.wait_ge(trans_done, t.k + 1)
                src = trans_ps[t.parity][:, :].rearrange("q (tg ph o) -> q ph o tg", ph=PH, o=CG)
                act.copy(c_T[t.parity][:, :, :].rearrange("q ph (o tg) -> q ph o tg", o=CG), src).then_inc(c_T_ready, 1)
                act.copy(c_hi[t.parity][:, :, :].rearrange("q ph (o tg) -> q ph o tg", o=CG), src).then_inc(c_hi_ready, 1)

            def keep_hw_hi(t):
                act.wait_ge(hw_trans_done, t.k + 1)
                wait(act, y_done, t.k - 1)
                act.copy(hw_hi[t.parity][:, :], low_ps[t.parity][:, HW_T]).then_inc(hw_hi_ready, 1)

            def step(t):
                exponentials(t)
                if t.after(1).exists(TILES):
                    keep_c(t.after(1))
                keep_hw_hi(t)

            keep_c(Tile(0))
            for_tiles(act, step, TILES, loop_first=1, rounds=3, unroll=4)

        @block.vector
        def _(dve):
            def split_phases(t):
                dve.wait_ge(x_loaded[t.parity], 16 * (t.before + 1))
                wait(dve, shuffled[t.parity], 16 * PH * t.before)
                dve.tensor_copy(x_ph[t.parity][:, :, :],
                                x_sb[:, t.k, :].rearrange("p (q ph) -> p ph q", ph=PH)).then_inc(by_phase, 1)

            def keep_conv(t):
                dve.wait_ge(conv_done, t.k + 1)
                wait(dve, trans_done, t.k - 1)
                add = ctx_T[:, bass.ds(T * t.k, T)].unsqueeze(2).to_broadcast([P, T, Q])
                dve.tensor_tensor(conv_sb[t.parity][:, :, :], conv_ps[t.parity][:, :].rearrange("p (t q) -> p t q", t=T),
                                  add, ALU.add).then_inc(conv_kept, 1)

            def route(t):
                def step_done(n):
                    dve.wait_ge(route_step, ROUTE_STEPS * t.k + n)

                def did(ins):
                    ins.then_inc(route_step, 1)

                dve.wait_ge(low_done, t.k + 1)
                did(dve.tensor_copy(logits[:, 0:E], low_ps[t.parity][:, LOGITS]))
                step_done(1)
                did(dve.tensor_reduce(neg_max[:, :], logits[:, 0:E], AX.X, ALU.max, negate=True))
                did(dve.max(ranked[:, :], logits[:, 0:E]))
                step_done(3)
                did(dve.tensor_copy(top2[:, 0:2], ranked[:, 0:2]))
                dve.wait_ge(exp_done, t.k + 1)
                step_done(4)
                did(dve.reciprocal(inv_total[:, :], total[:, :]))
                did(dve.match_replace(rest[:, :], top2[:, :], logits[:, :], TAKEN))
                step_done(6)
                did(dve.tensor_tensor(is_chosen[:, :], logits[:, 0:E], rest[:, 0:E], ALU.not_equal))
                step_done(7)
                did(dve.scalar_tensor_tensor(out=chosen[:, :], in0=expo[:, :], scalar=inv_total[:, :],
                                             in1=is_chosen[:, :], op0=ALU.mult, op1=ALU.mult,
                                             accum_out=chosen_sum[:, :]))
                step_done(8)
                did(dve.reciprocal(inv_chosen[:, :], chosen_sum[:, :]))
                step_done(9)
                wait(dve, hw_trans_done, t.k - 1)
                dve.scalar_tensor_tensor(
                    out=hw[t.parity][:, :].rearrange("p (e r) -> p e r", e=E),
                    in0=low_ps[t.parity][:, H].rearrange("p (e r) -> p e r", e=E), scalar=inv_chosen[:, :],
                    in1=chosen[:, :].unsqueeze(2).to_broadcast([P, E, R]), op0=ALU.mult, op1=ALU.mult).then_inc(hw_ready, 1)

            def finish(t):
                dve.wait_ge(y_done, t.k + 1)
                dve.wait_ge(biased, t.k + 1)
                wait(dve, stored[t.parity], 16 * t.before)
                dve.tensor_tensor(out_sb[t.parity][:, :], y_ps[t.parity][:, :], x_sb[:, t.k, :], ALU.add).then_inc(out_ready, 1)

            def keep_c_lo(t):
                dve.wait_ge(c_hi_ready, t.k + 1)
                src = trans_ps[t.parity][:, :].rearrange("q (tg ph o) -> q ph o tg", ph=PH, o=CG)
                hi = c_hi[t.parity][:, :, :].bitcast(F32).rearrange("q ph (o tg) -> q ph o tg", o=CG)
                dve.tensor_tensor(c_lo[t.parity][:, :, :].rearrange("q ph (o tg) -> q ph o tg", o=CG), src, hi,
                                  ALU.subtract).then_inc(c_lo_ready, 1)

            def keep_hw_lo(t):
                dve.wait_ge(hw_hi_ready, t.k + 1)
                dve.tensor_tensor(hw_lo[t.parity][:, :], low_ps[t.parity][:, HW_T], hw_hi[t.parity][:, :].bitcast(F32),
                                  ALU.subtract).then_inc(hw_lo_ready, 1)

            def step(t):
                if t.after(1).exists(TILES):
                    keep_conv(t.after(1))
                if t.after(-1).exists(TILES):
                    keep_hw_lo(t.after(-1))
                route(t)
                if t.after(-1).exists(TILES):
                    finish(t.after(-1))
                if t.after(1).exists(TILES):
                    keep_c_lo(t.after(1))
                if t.after(4).exists(TILES):
                    split_phases(t.after(4))

            for r in range(4):
                edges = win[r][ROWS:2 * ROWS, :].rearrange("p (tg j) -> p tg j", j=QP)
                dve.memset(edges[:, :, 0:1], 0.0)
                last = dve.memset(edges[:, :, QP - 1:QP], 0.0)
            last.then_inc(pads_zero, 1)
            dve.memset(taps_pad[:, :, :], 0.0).then_inc(taps_step, 1)
            dve.memset(logits[:, :], NOBODY).then_inc(taps_step, 1)
            dve.memset(top2[:, :], NOBODY)
            split_phases(Tile(0))
            split_phases(Tile(1))

            dve.wait_ge(taps_loaded, 16)
            dve.wait_ge(taps_step, 2)
            dve.tensor_copy(taps_pad[:, :, PH - 1:PH - 1 + TAPS], taps_nat[:, :, :]).then_inc(tap_order, 1)
            dve.wait_ge(tap_order, 1)
            for ph in range(PH):
                src = taps_pad[:, :, PH - 1 - ph:PH - 1 - ph + BLK * PH].rearrange("o c (a b) -> o a b c", a=BLK)
                last = dve.tensor_copy(taps_win[:, :, ph, :, :], src)
            last.then_inc(tap_order, 1)
            dve.wait_ge(tap_order, 2)
            dve.transpose(taps_T[:, :, :, :].rearrange("p a h o -> p (a h o)"),
                          taps_win[:, :, :, :, :].rearrange("o a h b c -> o (a h b c)")).then_inc(tap_order, 1)
            dve.wait_ge(tap_order, 3)
            for a in range(BLK):
                src = taps_T[:, a, :, :].rearrange("p h (g o) -> p g h o", g=G)
                last = dve.tensor_copy(conv_lhs[a * ROWS:(a + 1) * ROWS, :, :, :], src)
            last.then_inc(taps_step, 1)

            def keep_lo(lo, hi, ps, n):
                dve.wait_ge(prep_kept, n)
                dve.tensor_tensor(lo, ps, hi.bitcast(F32), ALU.subtract).then_inc(prep_lo, 1)

            def keep_w_lo(ph):
                keep_lo(w_lo[:, ph, :], w_hi[:, ph, :], bank[W_BANKS[ph]][:, :], 3 + ph)

            split_phases(Tile(2))
            keep_w_lo(0)
            keep_w_lo(1)
            split_phases(Tile(3))
            keep_w_lo(2)
            keep_w_lo(3)
            dve.wait_ge(prep_kept, 8)
            keep_conv(Tile(0))
            keep_lo(b_lo[:, :].rearrange("k (p ob) -> k ob p", ob=OB), b_hi[:, :].rearrange("k (p ob) -> k ob p", ob=OB),
                    bank[B_BANK][:, :].rearrange("k (ob p) -> k ob p", ob=OB), 9)
            keep_c_lo(Tile(0))
            for_tiles(dve, step, TILES, loop_first=4, rounds=4, unroll=2)
            keep_hw_lo(Tile(TILES - 1))
            finish(Tile(TILES - 1))


_INS = ["x", "cond_128", "fside_S_0", "L0_cond_weight", "L0_cond_c_weight", "L0_ffn_W_base", "L0_ffn_b_base",
        "L0_ffn_W_gate", "L0_ffn_A", "L0_ffn_B"]


def kernel(**inputs):
    import numpy as _np
    import concourse.bacc as _bacc
    from concourse.bass_utils import run_bass_kernel_spmd as _run

    nc = _bacc.Bacc("TRN2", target_bir_lowering=False, num_devices=1)
    arrays, args = {}, []
    for name in _INS:
        a = _np.ascontiguousarray(inputs[name])
        arrays[f"in_{name}_dram"] = a
        args.append(nc.dram_tensor(f"in_{name}_dram", a.shape, mybir.dt.from_np(a.dtype), kind="ExternalInput").ap())
    shape = inputs["x"].shape
    args.append(nc.dram_tensor("out_0_dram", shape, F32, kind="ExternalOutput").ap())
    build(nc, *args)
    r = _run(nc, [arrays], core_ids=[0])
    return r.results[0]["out_0_dram"]
```

```python
from contextlib import ExitStack

import concourse.bass as bass
from concourse import mybir

ALU = mybir.AluOpType
ACT = mybir.ActivationFunctionType
AX = mybir.AxisListType
F32 = mybir.dt.float32
F32R = mybir.dt.float32r

P = 128


class Tile:

    def __init__(self, j, round=0, unroll=4):
        self.j, self.round, self.unroll = j, round, unroll
        self.k = unroll * round + j
        self.parity, self.slot = j % 2, j % 4
        self.before = unroll // 2 * round + j // 2
        self.laps = unroll // 4 * round + j // 4

    def after(self, n):
        return Tile(self.j + n, self.round, self.unroll)

    def exists(self, tiles):
        return not isinstance(self.k, int) or 0 <= self.k < tiles


def for_tiles(eng, step, tiles, loop_first, rounds, unroll, first=0):
    for k in range(first, loop_first):
        step(Tile(k))
    with eng.Fori(0, rounds) as round:
        for j in range(unroll):
            step(Tile(loop_first + j, round, unroll))
    for k in range(loop_first + rounds * unroll, tiles):
        step(Tile(k))


def wait(eng, semaphore, value):
    if not isinstance(value, int) or value > 0:
        eng.wait_ge(semaphore, value)


def build(nc, x, cond, bias, conv_w, ctx_w, w_base, b_base, w_gate, lora_a, lora_b, out):
    N, CH, L = x.shape
    _, CG, TAPS = conv_w.shape
    G = CH // CG
    COND = cond.shape[1]
    OUT = w_base.shape[0]
    E, R, _ = lora_a.shape
    ER = E * R
    PH = 4
    Q = L // PH
    T = P // CH
    TG = T * G
    TILES = N // T
    BLK = (PH + TAPS - 1) // PH
    ROWS = PH * CG
    QP = Q + 2
    OB = OUT // P
    PADW = PH * BLK + PH
    NOBODY = -3.0e38
    TAKEN = 3.0e38
    EARLY = 3
    STORE_LAG = 5
    assert (Q, T, BLK, ROWS, E, ER, COND, OUT) == (P, 4, 3, 32, 8, P, P, 4 * P) and TILES % 2 == 0

    x_rows = x.rearrange("n c l -> (n c) l").rearrange("(k tg c) l -> k c tg l", tg=TG, c=CG)
    out_rows = out.rearrange("n c l -> (n c) l").rearrange("(k tg c) l -> k c tg l", tg=TG, c=CG)

    with ExitStack() as ctx:
        def sb(name, shape, dtype=F32):
            return ctx.enter_context(nc.sbuf_tensor(name, shape, dtype))

        def sem(name):
            return ctx.enter_context(nc.semaphore(name))

        def pair(name):
            return [sem(f"{name}_even"), sem(f"{name}_odd")]

        x_sb = sb("x_sb", [P, TILES, L])
        x_ph = [sb(f"x_ph{r}", [P, PH, Q]) for r in range(2)]
        win = [sb(f"win{r}", [P, TG * QP]) for r in range(4)]
        conv_sb = [sb(f"conv_sb{r}", [P, T, Q]) for r in range(2)]
        c_T = [sb(f"c_T{r}", [P, PH, P]) for r in range(2)]
        c_hi = [sb(f"c_hi{r}", [P, PH, P], F32R) for r in range(2)]
        c_lo = [sb(f"c_lo{r}", [P, PH, P], F32R) for r in range(2)]
        hw = [sb(f"hw{r}", [P, ER]) for r in range(2)]
        hw_hi = [sb(f"hw_hi{r}", [P, P], F32R) for r in range(2)]
        hw_lo = [sb(f"hw_lo{r}", [P, P], F32R) for r in range(2)]
        out_sb = [sb(f"out_sb{r}", [P, OUT]) for r in range(2)]
        neg_max = sb("neg_max", [P, 1])
        expo = sb("expo", [P, E])
        total = sb("total", [P, 1])
        inv_total = sb("inv_total", [P, 1])
        logits = sb("logits", [P, 2 * E])
        ranked = sb("ranked", [P, E])
        top2 = sb("top2", [P, E])
        rest = sb("rest", [P, 2 * E])
        is_chosen = sb("is_chosen", [P, E])
        chosen = sb("chosen", [P, E])
        chosen_sum = sb("chosen_sum", [P, 1])
        inv_chosen = sb("inv_chosen", [P, 1])
        ident = sb("ident", [P, P])
        ones = sb("ones", [1, N])
        b_bc = sb("b_bc", [P, OUT])
        w_nat = sb("w_nat", [P, OB, L])
        a_nat = sb("a_nat", [P, L])
        gate_nat = sb("gate_nat", [E, L])
        b_nat = sb("b_nat", [P, E, OB, R])
        b_ob = sb("b_ob", [P, OB, E, R])
        cond_nat = sb("cond_nat", [N, COND])
        ctxw_nat = sb("ctxw_nat", [CH, COND])
        bias_rep = sb("bias_rep", [1, G, PH, CG])
        taps_nat = sb("taps_nat", [CH, CG, TAPS])
        taps_pad = sb("taps_pad", [CH, CG, PADW])
        taps_win = sb("taps_win", [CH, BLK, PH, PH, CG])
        taps_T = sb("taps_T", [ROWS, BLK, PH, CH])
        conv_lhs = sb("conv_lhs", [P, G, PH, CG])
        w_hi = sb("w_hi", [P, PH, OUT], F32R)
        w_lo = sb("w_lo", [P, PH, OUT], F32R)
        ag_T = sb("ag_T", [P, PH, ER + E])
        b_hi = sb("b_hi", [P, OUT], F32R)
        b_lo = sb("b_lo", [P, OUT], F32R)
        cond_T = sb("cond_T", [COND, N])
        ctxw_rep = sb("ctxw_rep", [COND, G, PH, CG])
        ctx_T = sb("ctx_T", [P, N])

        bank = [ctx.enter_context(nc.psum_tensor(f"bank{i}", [P, 512], F32)) for i in range(8)]
        conv_ps, trans_ps, low_ps, y_ps = bank[0:2], bank[2:4], bank[4:6], bank[6:8]
        A_BANK, CTX_BANK, GATE_BANK, W_BANKS, B_BANK = 3, 2, 1, (4, 5, 6, 7), 7
        A_FULL, COND_FULL, CTX_FULL, GATE_FULL, W_FULL, B_FULL = 1, 2, 3, 4, 5, 5 + PH
        H = slice(0, ER)
        LOGITS = slice(ER, ER + E)
        HW_T = slice(2 * P, 3 * P)

        x_loaded, shuffled, stored = pair("x_loaded"), pair("shuffled"), pair("stored")
        windowed = [sem(f"windowed{r}") for r in range(4)]
        windowed_early = [sem(f"windowed_early{r}") for r in range(EARLY)]
        w_loaded, w_half_loaded, a_loaded = sem("w_loaded"), sem("w_half_loaded"), sem("a_loaded")
        gate_loaded, b_loaded = sem("gate_loaded"), sem("b_loaded")
        b_ordered = sem("b_ordered")
        ctx_loaded, taps_loaded, bb_loaded = sem("ctx_loaded"), sem("taps_loaded"), sem("bb_loaded")
        ident_step, pads_zero, preset = sem("ident_step"), sem("pads_zero"), sem("preset")
        taps_step, tap_order = sem("taps_step"), sem("tap_order")
        prep_done, prep_kept = sem("prep_done"), sem("prep_kept")
        prep_lo = sem("prep_lo")
        by_phase, conv_done, conv_kept = sem("by_phase"), sem("conv_done"), sem("conv_kept")
        trans_done, c_T_ready = sem("trans_done"), sem("c_T_ready")
        c_hi_ready, c_lo_ready = sem("c_hi_ready"), sem("c_lo_ready")
        low_done, exp_done, route_step, hw_ready = sem("low_done"), sem("exp_done"), sem("route_step"), sem("hw_ready")
        hw_trans_done, hw_hi_ready, hw_lo_ready = sem("hw_trans_done"), sem("hw_hi_ready"), sem("hw_lo_ready")
        y_done, out_ready, biased = sem("y_done"), sem("out_ready"), sem("biased")
        ROUTE_STEPS = 9

        block = ctx.enter_context(nc.Block())

        w_rows = w_base.rearrange("(ob p) l -> p ob l", p=P)

        def is_first(t):
            return isinstance(t.k, int) and t.k == 0

        def is_early(t):
            return isinstance(t.k, int) and t.k < EARLY

        def shift_window(eng, t):
            w, done = win[t.slot], windowed_early[t.slot] if is_early(t) else windowed[t.slot]
            eng.dma_start(w[0:ROWS, 1:], w[ROWS:2 * ROWS, :-1]).then_inc(done, 16)
            eng.dma_start(w[2 * ROWS:3 * ROWS, :-1], w[ROWS:2 * ROWS, 1:]).then_inc(done, 16)

        def early_shift(eng, t):
            eng.wait_ge(shuffled[t.parity], 16 * PH * (t.before + 1))
            shift_window(eng, t)

        @block.sync
        def _(sp):
            def load_x(t):
                sp.dma_start(x_sb[:, t.k, :], x_rows[t.k]).then_inc(x_loaded[t.parity], 16)

            def shuffle(t, phases=range(PH)):
                wait(sp, conv_done, t.k - 3)
                for b in phases:
                    rows = win[t.slot][ROWS + b * CG:ROWS + (b + 1) * CG, :].rearrange("c (tg j) -> c tg j", j=QP)
                    sp.dma_start(rows[:, :, 1:1 + Q], x_ph[t.parity][:, b, :]).then_inc(shuffled[t.parity], 16)

            def store(t):
                sp.wait_ge(out_ready, t.k + 1)
                sp.dma_start(out_rows[t.k], out_sb[t.parity][:, :]).then_inc(stored[t.parity], 16)

            def step(t):
                sp.wait_ge(by_phase, t.k + 1)
                at_start = isinstance(t.k, int) and t.k <= STORE_LAG
                if at_start:
                    shuffle(t)
                if t.after(2).exists(TILES):
                    load_x(t.after(2))
                if t.after(-STORE_LAG).exists(TILES):
                    store(t.after(-STORE_LAG))
                if not at_start:
                    shuffle(t)

            def early_shuffle(t, phases=range(PH)):
                sp.wait_ge(by_phase, t.k + 1)
                shuffle(t, phases)

            load_x(Tile(0))
            load_x(Tile(1))
            sp.wait_ge(pads_zero, 1)
            early_shuffle(Tile(0))
            load_x(Tile(2))
            early_shuffle(Tile(1))
            early_shuffle(Tile(2), range(0, PH // 2))
            early_shift(sp, Tile(1))
            early_shuffle(Tile(2), range(PH // 2, PH))
            load_x(Tile(3))
            sp.dma_start(b_nat[:, :, :, :], lora_b.rearrange("e (p ob) r -> p e (ob r)", ob=OB)).then_inc(b_loaded, 16)
            load_x(Tile(4))
            for_tiles(sp, step, TILES, loop_first=STORE_LAG + 1, rounds=2, unroll=4, first=EARLY)
            for k in range(TILES - STORE_LAG, TILES):
                store(Tile(k))
            for r in range(2):
                sp.wait_ge(stored[r], 16 * TILES // 2)

        @block.gpsimd
        def _(pool):
            pool.memset(ident[:, :], 0.0).then_inc(ident_step, 1)
            pool.wait_ge(ident_step, 1)
            pool.affine_select(out=ident[:, :], in_=ident[:, :], compare_op=ALU.not_equal, fill=1.0, base=0,
                               pattern=[[-1, P]], channel_multiplier=1).then_inc(ident_step, 1)
            pool.wait_ge(ident_step, 2)
            pool.memset(ones[:, :], 1.0).then_inc(preset, 1)
            pool.wait_ge(preset, 1)
            pool.dma_start(cond_nat[:, :], cond).then_inc(ctx_loaded, 16)
            pool.dma_start(ctxw_nat[:, :], ctx_w).then_inc(ctx_loaded, 16)
            bias_src = bias.rearrange("(a g s o) -> a g s o", a=1, g=G, s=1).to_broadcast([1, G, PH, CG])
            pool.dma_start(bias_rep[:, :, :, :], bias_src).then_inc(ctx_loaded, 16)
            pool.dma_start(w_nat[:, OB // 2:OB, :], w_rows[:, OB // 2:OB, :]).then_inc(w_half_loaded, 16)
            pool.dma_start(gate_nat[:, :], w_gate).then_inc(gate_loaded, 16)
            b_base_src = b_base.rearrange("(a o) -> a o", a=1).to_broadcast([P, OUT])
            pool.dma_start(b_bc[:, :], b_base_src).then_inc(bb_loaded, 16)
            early_shift(pool, Tile(2))
            pool.wait_ge(bb_loaded, 16)

            def step(t):
                def add_b_base(lo, hi):
                    part = x_sb[:, t.k, lo:hi]
                    pool.tensor_tensor(part, part, b_bc[:, lo:hi], ALU.add).then_inc(biased, 1)

                pool.wait_ge(by_phase, t.k + 1)
                pool.wait_ge(shuffled[t.parity], 16 * PH * (t.before + 1))
                add_b_base(0, Q // 2)
                if not is_early(t):
                    shift_window(pool, t)
                add_b_base(Q // 2, OUT)

            for_tiles(pool, step, TILES, loop_first=4, rounds=3, unroll=4)

        @block.tensor
        def _(pe):
            pe.wait_ge(ident_step, 2)
            w_ph = w_nat[:, :, :].rearrange("p ob (q ph) -> p ob q ph", ph=PH)
            a_ph = a_nat[:, :].rearrange("p (q ph) -> p q ph", ph=PH)
            gate_ph = gate_nat[:, :].rearrange("p (q ph) -> p q ph", ph=PH)

            pe.wait_ge(a_loaded, 16)
            for ph in range(PH):
                last = pe.transpose(bank[A_BANK][:, ph * P:(ph + 1) * P], a_ph[:, :, ph], ident[:, :])
            last.then_inc(prep_done, 1)
            pe.wait_ge(ctx_loaded, 48)
            pe.transpose(bank[CTX_BANK][:, 0:N], cond_nat[:, :], ident[0:N, 0:N])
            pe.transpose(bank[CTX_BANK][:, N:N + CH], ctxw_nat[:, :], ident[0:CH, 0:CH]).then_inc(prep_done, 1)
            pe.wait_ge(prep_kept, COND_FULL)
            pe.wait_ge(preset, 1)
            pe.matmul(bank[CTX_BANK][:, 0:N], ctxw_rep[:, :, :, :], cond_T[:, :], start=True, stop=False)
            pe.matmul(bank[CTX_BANK][:, 0:N], bias_rep[:, :, :, :], ones[:, :],
                      start=False, stop=True).then_inc(prep_done, 1)

            pe.wait_ge(gate_loaded, 16)
            for ph in range(PH):
                last = pe.transpose(bank[GATE_BANK][:, ph * E:(ph + 1) * E], gate_ph[:, :, ph], ident[0:E, 0:E])
            last.then_inc(prep_done, 1)
            pe.wait_ge(w_loaded, 16)
            pe.wait_ge(w_half_loaded, 16)
            for ph in range(PH):
                for ob in range(OB):
                    last = pe.transpose(bank[W_BANKS[ph]][:, ob * P:(ob + 1) * P], w_ph[:, ob, :, ph], ident[:, :])
                last.then_inc(prep_done, 1)

            def transpose_b():
                pe.wait_ge(b_ordered, 1)
                pe.wait_ge(prep_lo, PH)
                for ob in range(OB):
                    last = pe.transpose(bank[B_BANK][:, ob * P:(ob + 1) * P], b_ob[:, ob, :, :], ident[:, :])
                last.then_inc(prep_done, 1)

            def convolve(t):
                if is_early(t):
                    pe.wait_ge(windowed_early[t.slot], 32)
                else:
                    pe.wait_ge(windowed[t.slot], 32 * (t.laps + 1 - (t.slot < EARLY)))
                wait(pe, conv_kept, t.k - 1)
                rows = win[t.slot][0:BLK * ROWS, :].rearrange("p (t g j) -> p t g j", g=G, j=QP)
                for g in range(G):
                    last = pe.matmul(conv_ps[t.parity][g * 32:(g + 1) * 32, :], conv_lhs[0:BLK * ROWS, g, :, :],
                                     rows[:, :, g, 1:1 + Q], start=True, stop=True)
                last.then_inc(conv_done, 1)

            def transpose_c(t):
                pe.wait_ge(conv_kept, t.k + 1)
                wait(pe, c_hi_ready, t.k - 1)
                wait(pe, c_lo_ready, t.k - 1)
                for s in range(T):
                    last = pe.transpose(trans_ps[t.parity][:, s * P:(s + 1) * P], conv_sb[t.parity][:, s, :],
                                        ident[:, :])
                last.then_inc(trans_done, 1)

            def low_rank(t):
                pe.wait_ge(c_T_ready, t.k + 1)
                wait(pe, hw_lo_ready, t.k - 1)
                for ph in range(PH):
                    last = pe.matmul(low_ps[t.parity][:, 0:ER + E], c_T[t.parity][:, ph, :], ag_T[:, ph, :],
                                     start=(ph == 0), stop=(ph == PH - 1))
                last.then_inc(low_done, 1)

            def transpose_hw(t):
                pe.wait_ge(hw_ready, t.k + 1)
                pe.transpose(low_ps[t.parity][:, HW_T], hw[t.parity][:, :], ident[:, :]).then_inc(hw_trans_done, 1)

            def base(t):
                y, hi, lo = y_ps[t.parity], c_hi[t.parity], c_lo[t.parity]
                wait(pe, out_ready, t.k - 1)
                pe.wait_ge(c_hi_ready, t.k + 1)
                for ph in range(PH):
                    pe.matmul(y[:, :], hi[:, ph, :], w_hi[:, ph, :], start=(ph == 0), stop=False)
                    pe.matmul(y[:, :], hi[:, ph, :], w_lo[:, ph, :], start=False, stop=False)
                if not is_first(t):
                    transpose_hw(t)
                pe.wait_ge(c_lo_ready, t.k + 1)
                for ph in range(PH):
                    pe.matmul(y[:, :], lo[:, ph, :], w_hi[:, ph, :], start=False, stop=False)
                if is_first(t):
                    transpose_hw(t)

            def experts(t):
                y, hi, lo = y_ps[t.parity], hw_hi[t.parity], hw_lo[t.parity]
                pe.wait_ge(hw_hi_ready, t.k + 1)
                pe.matmul(y[:, :], hi[:, :], b_hi[:, :], start=False, stop=False)
                pe.matmul(y[:, :], hi[:, :], b_lo[:, :], start=False, stop=False)
                pe.wait_ge(hw_lo_ready, t.k + 1)
                pe.matmul(y[:, :], lo[:, :], b_hi[:, :], start=False, stop=True).then_inc(y_done, 1)

            def step(t):
                low_rank(t)
                if t.after(-1).exists(TILES):
                    if is_first(t.after(-1)):
                        pe.wait_ge(prep_lo, PH + 1)
                    experts(t.after(-1))
                if t.after(1).exists(TILES):
                    transpose_c(t.after(1))
                base(t)
                if is_first(t):
                    transpose_b()
                if t.after(2).exists(TILES):
                    convolve(t.after(2))

            pe.wait_ge(taps_step, 3)
            convolve(Tile(0))
            transpose_c(Tile(0))
            convolve(Tile(1))
            pe.wait_ge(prep_lo, PH)
            for_tiles(pe, step, TILES, loop_first=2, rounds=3, unroll=4)
            experts(Tile(TILES - 1))

        @block.scalar
        def _(act):
            act.dma_start(taps_nat[:, :, :], conv_w).then_inc(taps_loaded, 16)
            act.dma_start(a_nat[:, :], lora_a.rearrange("e r l -> (e r) l")).then_inc(a_loaded, 16)
            act.dma_start(w_nat[:, 0:OB // 2, :], w_rows[:, 0:OB // 2, :]).then_inc(w_loaded, 16)

            act.wait_ge(prep_done, A_FULL)
            act.copy(ag_T[:, :, 0:ER], bank[A_BANK][:, :].rearrange("q (ph e) -> q ph e", ph=PH)).then_inc(prep_kept, 1)
            act.wait_ge(prep_done, COND_FULL)
            act.copy(cond_T[:, :], bank[CTX_BANK][:, 0:N])
            cw = bank[CTX_BANK][:, N:N + CH].rearrange("d (g s o) -> d g s o", g=G, s=1).to_broadcast([COND, G, PH, CG])
            act.copy(ctxw_rep[:, :, :, :], cw).then_inc(prep_kept, 1)
            act.wait_ge(prep_done, CTX_FULL)
            act.copy(ctx_T[:, :], bank[CTX_BANK][:, 0:N]).then_inc(prep_kept, 1)
            early_shift(act, Tile(0))
            act.wait_ge(prep_done, GATE_FULL)
            act.copy(ag_T[:, :, ER:ER + E],
                     bank[GATE_BANK][:, 0:PH * E].rearrange("q (ph e) -> q ph e", ph=PH)).then_inc(prep_kept, 1)
            for ph in range(PH):
                act.wait_ge(prep_done, W_FULL + ph)
                act.copy(w_hi[:, ph, :], bank[W_BANKS[ph]][:, :]).then_inc(prep_kept, 1)

            def exponentials(t):
                act.wait_ge(route_step, ROUTE_STEPS * t.k + 2)
                act.activation(expo[:, :], low_ps[t.parity][:, LOGITS], ACT.Exp, bias=neg_max[:, :],
                               accum_out=total[:, :]).then_inc(exp_done, 1)

            def keep_c(t):
                act.wait_ge(trans_done, t.k + 1)
                src = trans_ps[t.parity][:, :].rearrange("q (tg ph o) -> q ph o tg", ph=PH, o=CG)
                whole = c_T[t.parity][:, :, :].rearrange("q ph (o tg) -> q ph o tg", o=CG)
                hi = c_hi[t.parity][:, :, :].rearrange("q ph (o tg) -> q ph o tg", o=CG)
                act.copy(whole, src).then_inc(c_T_ready, 1)
                act.copy(hi, src).then_inc(c_hi_ready, 1)

            def keep_hw_hi(t):
                act.wait_ge(hw_trans_done, t.k + 1)
                wait(act, y_done, t.k - 1)
                act.copy(hw_hi[t.parity][:, :], low_ps[t.parity][:, HW_T]).then_inc(hw_hi_ready, 1)

            def step(t):
                exponentials(t)
                if t.after(1).exists(TILES):
                    keep_c(t.after(1))
                if is_first(t):
                    act.wait_ge(b_loaded, 16)
                    by_output = b_nat[:, :, :, :].rearrange("p e ob r -> p ob e r")
                    act.copy(b_ob[:, :, :, :], by_output).then_inc(b_ordered, 1)
                keep_hw_hi(t)
                if is_first(t):
                    act.wait_ge(prep_done, B_FULL)
                    act.copy(b_hi[:, :].rearrange("k (p ob) -> k ob p", ob=OB),
                             bank[B_BANK][:, :].rearrange("k (ob p) -> k ob p", ob=OB)).then_inc(prep_kept, 1)

            keep_c(Tile(0))
            for_tiles(act, step, TILES, loop_first=2, rounds=3, unroll=4)

        @block.vector
        def _(dve):
            def split_phases(t):
                dve.wait_ge(x_loaded[t.parity], 16 * (t.before + 1))
                wait(dve, shuffled[t.parity], 16 * PH * t.before)
                dve.tensor_copy(x_ph[t.parity][:, :, :],
                                x_sb[:, t.k, :].rearrange("p (q ph) -> p ph q", ph=PH)).then_inc(by_phase, 1)

            def keep_conv(t):
                dve.wait_ge(conv_done, t.k + 1)
                wait(dve, trans_done, t.k - 1)
                add = ctx_T[:, bass.ds(T * t.k, T)].unsqueeze(2).to_broadcast([P, T, Q])
                dve.tensor_tensor(conv_sb[t.parity][:, :, :], conv_ps[t.parity][:, :].rearrange("p (t q) -> p t q", t=T),
                                  add, ALU.add).then_inc(conv_kept, 1)

            def route(t):
                def step_done(n):
                    dve.wait_ge(route_step, ROUTE_STEPS * t.k + n)

                def did(ins):
                    ins.then_inc(route_step, 1)

                dve.wait_ge(low_done, t.k + 1)
                did(dve.tensor_copy(logits[:, 0:E], low_ps[t.parity][:, LOGITS]))
                step_done(1)
                did(dve.tensor_reduce(neg_max[:, :], logits[:, 0:E], AX.X, ALU.max, negate=True))
                did(dve.max(ranked[:, :], logits[:, 0:E]))
                step_done(3)
                did(dve.tensor_copy(top2[:, 0:2], ranked[:, 0:2]))
                dve.wait_ge(exp_done, t.k + 1)
                step_done(4)
                did(dve.reciprocal(inv_total[:, :], total[:, :]))
                did(dve.match_replace(rest[:, :], top2[:, :], logits[:, :], TAKEN))
                step_done(6)
                did(dve.tensor_tensor(is_chosen[:, :], logits[:, 0:E], rest[:, 0:E], ALU.not_equal))
                step_done(7)
                did(dve.scalar_tensor_tensor(out=chosen[:, :], in0=expo[:, :], scalar=inv_total[:, :],
                                             in1=is_chosen[:, :], op0=ALU.mult, op1=ALU.mult,
                                             accum_out=chosen_sum[:, :]))
                step_done(8)
                did(dve.reciprocal(inv_chosen[:, :], chosen_sum[:, :]))
                step_done(9)
                wait(dve, hw_trans_done, t.k - 1)
                dve.scalar_tensor_tensor(
                    out=hw[t.parity][:, :].rearrange("p (e r) -> p e r", e=E),
                    in0=low_ps[t.parity][:, H].rearrange("p (e r) -> p e r", e=E), scalar=inv_chosen[:, :],
                    in1=chosen[:, :].unsqueeze(2).to_broadcast([P, E, R]), op0=ALU.mult, op1=ALU.mult).then_inc(hw_ready, 1)

            def finish(t):
                dve.wait_ge(y_done, t.k + 1)
                dve.wait_ge(biased, 2 * t.k + 2)
                wait(dve, stored[t.parity], 16 * t.before)
                dve.tensor_tensor(out_sb[t.parity][:, :], y_ps[t.parity][:, :], x_sb[:, t.k, :],
                                  ALU.add).then_inc(out_ready, 1)

            def keep_c_lo(t):
                dve.wait_ge(c_hi_ready, t.k + 1)
                src = trans_ps[t.parity][:, :].rearrange("q (tg ph o) -> q ph o tg", ph=PH, o=CG)
                hi = c_hi[t.parity][:, :, :].bitcast(F32).rearrange("q ph (o tg) -> q ph o tg", o=CG)
                dve.tensor_tensor(c_lo[t.parity][:, :, :].rearrange("q ph (o tg) -> q ph o tg", o=CG), src, hi,
                                  ALU.subtract).then_inc(c_lo_ready, 1)

            def keep_hw_lo(t):
                dve.wait_ge(hw_hi_ready, t.k + 1)
                dve.tensor_tensor(hw_lo[t.parity][:, :], low_ps[t.parity][:, HW_T], hw_hi[t.parity][:, :].bitcast(F32),
                                  ALU.subtract).then_inc(hw_lo_ready, 1)

            def keep_lo(lo, hi, ps, n):
                dve.wait_ge(prep_kept, n)
                dve.tensor_tensor(lo, ps, hi.bitcast(F32), ALU.subtract).then_inc(prep_lo, 1)

            def keep_w_lo(ph):
                keep_lo(w_lo[:, ph, :], w_hi[:, ph, :], bank[W_BANKS[ph]][:, :], W_FULL + ph)

            def keep_b_lo():
                keep_lo(b_lo[:, :].rearrange("k (p ob) -> k ob p", ob=OB), b_hi[:, :].rearrange("k (p ob) -> k ob p", ob=OB),
                        bank[B_BANK][:, :].rearrange("k (ob p) -> k ob p", ob=OB), B_FULL)

            def step(t):
                if t.after(-1).exists(TILES):
                    keep_hw_lo(t.after(-1))
                route(t)
                if t.after(-1).exists(TILES):
                    finish(t.after(-1))
                if t.after(1).exists(TILES):
                    keep_c_lo(t.after(1))
                if t.after(4).exists(TILES):
                    split_phases(t.after(4))
                if is_first(t):
                    keep_b_lo()
                if t.after(2).exists(TILES):
                    keep_conv(t.after(2))

            for r in range(4):
                edges = win[r][ROWS:2 * ROWS, :].rearrange("p (tg j) -> p tg j", j=QP)
                dve.memset(edges[:, :, 0:1], 0.0)
                last = dve.memset(edges[:, :, QP - 1:QP], 0.0)
            last.then_inc(pads_zero, 1)
            dve.memset(taps_pad[:, :, :], 0.0).then_inc(taps_step, 1)
            dve.memset(logits[:, :], NOBODY).then_inc(taps_step, 1)
            dve.memset(top2[:, :], NOBODY)
            split_phases(Tile(0))
            split_phases(Tile(1))

            dve.wait_ge(taps_loaded, 16)
            dve.wait_ge(taps_step, 2)
            dve.tensor_copy(taps_pad[:, :, PH - 1:PH - 1 + TAPS], taps_nat[:, :, :]).then_inc(tap_order, 1)
            dve.wait_ge(tap_order, 1)
            for ph in range(PH):
                src = taps_pad[:, :, PH - 1 - ph:PH - 1 - ph + BLK * PH].rearrange("o c (a b) -> o a b c", a=BLK)
                last = dve.tensor_copy(taps_win[:, :, ph, :, :], src)
            last.then_inc(tap_order, 1)
            dve.wait_ge(tap_order, 2)
            dve.transpose(taps_T[:, :, :, :].rearrange("p a h o -> p (a h o)"),
                          taps_win[:, :, :, :, :].rearrange("o a h b c -> o (a h b c)")).then_inc(tap_order, 1)
            dve.wait_ge(tap_order, 3)
            for a in range(BLK):
                src = taps_T[:, a, :, :].rearrange("p h (g o) -> p g h o", g=G)
                last = dve.tensor_copy(conv_lhs[a * ROWS:(a + 1) * ROWS, :, :, :], src)
            last.then_inc(taps_step, 1)

            split_phases(Tile(2))
            keep_w_lo(0)
            keep_w_lo(1)
            keep_w_lo(2)
            keep_w_lo(3)
            keep_conv(Tile(0))
            keep_conv(Tile(1))
            split_phases(Tile(3))
            keep_c_lo(Tile(0))
            for_tiles(dve, step, TILES, loop_first=4, rounds=4, unroll=2)
            keep_hw_lo(Tile(TILES - 1))
            finish(Tile(TILES - 1))


_INS = ["x", "cond_128", "fside_S_0", "L0_cond_weight", "L0_cond_c_weight", "L0_ffn_W_base", "L0_ffn_b_base",
        "L0_ffn_W_gate", "L0_ffn_A", "L0_ffn_B"]


def kernel(**inputs):
    import numpy as _np
    import concourse.bacc as _bacc
    from concourse.bass_utils import run_bass_kernel_spmd as _run

    nc = _bacc.Bacc("TRN2", target_bir_lowering=False, num_devices=1)
    arrays, args = {}, []
    for name in _INS:
        a = _np.ascontiguousarray(inputs[name])
        arrays[f"in_{name}_dram"] = a
        args.append(nc.dram_tensor(f"in_{name}_dram", a.shape, mybir.dt.from_np(a.dtype), kind="ExternalInput").ap())
    shape = inputs["x"].shape
    args.append(nc.dram_tensor("out_0_dram", shape, F32, kind="ExternalOutput").ap())
    build(nc, *args)
    r = _run(nc, [arrays], core_ids=[0])
    return r.results[0]["out_0_dram"]
```
